# Optimizing a Trainium2 kernel written in Bass

```python
import numpy as np
import jax
import jax.numpy as jnp

def _softmax(x, axis=-1):
    return jax.nn.softmax(x, axis=axis)

def _gelu(x):
    return jax.nn.gelu(x, approximate=True)

def _silu(x):
    return jax.nn.silu(x)

def _sigmoid(x):
    return jax.nn.sigmoid(x)

def _layernorm(x, axis=-1, eps=1e-05):
    m = jnp.mean(x, axis=axis, keepdims=True)
    v = jnp.var(x, axis=axis, keepdims=True)
    return (x - m) / jnp.sqrt(v + eps)

def _scatter_add(tgt, idx, src, axis=0):
    return tgt.at[idx].add(src)

def _segment_sum(src, seg, n):
    return jax.ops.segment_sum(src, seg, n)
kernel_name = 'mk_adj_preln_d1_adj_r2_c011bf'

def setup_inputs(seed: int=0):
    np.random.seed(seed)
    _w = jnp.asarray

    def _rec_inputs():
        import jax
        import jax.numpy as jnp
        _gk = jax.random.key(seed)
        x = 7.22e-05 + 1 * jax.random.normal(jax.random.fold_in(_gk, 1), (8, 1024, 512), jnp.float32)
        _w = (1.0 + jnp.arange(1024, dtype=jnp.float32)) ** (-0.5)
        _w = _w / _w.mean()
        _pij = jnp.clip(0.00390625 * _w[:, None] * _w[None, :], 0.0, 1.0)
        _a = jax.random.uniform(jax.random.fold_in(_gk, 2), (1024, 1024)) < _pij
        _a = jnp.logical_or(_a, jnp.eye(1024, dtype=bool))
        _af = _a.astype(jnp.float32)
        adj = _af
        return (x, adj)
    x, adj = _rec_inputs()

    def _L0_gnn_setup():
        import jax, jax.numpy as jnp
        import numpy as np
        EPS = 1e-08

        def _row_stochastic_causal(A, causal_mask):
            A = A * causal_mask
            deg = jnp.maximum(A.sum(axis=-1, keepdims=True), EPS)
            return A / deg
        key = jax.random.key(seed)
        k = jax.random.split(key, 5)
        B, N, D = (4, 1024, 512)
        s = 1.0 / np.sqrt(D)
        h = jax.random.normal(k[0], (B, N, D), dtype=jnp.float32)
        W_lang = jax.random.normal(k[1], (D, D), dtype=jnp.float32) * s
        W_grav = jax.random.normal(k[2], (D, D), dtype=jnp.float32) * s
        W_V = jax.random.normal(k[3], (D, D), dtype=jnp.float32) * s
        W_O = jax.random.normal(k[4], (D, D), dtype=jnp.float32) * s
        causal_mask = jnp.tril(jnp.ones((N, N), dtype=jnp.float32))
        gate_logit = jnp.zeros((), jnp.float32)
        log_sigma = jnp.zeros((), jnp.float32)
        return {'h': h, 'causal_mask': causal_mask, 'W_lang': W_lang, 'W_grav': W_grav, 'W_V': W_V, 'W_O': W_O, 'gate_logit': gate_logit, 'log_sigma': log_sigma}
    _L0_gnn_all = _L0_gnn_setup()
    _L0_gnn_in = {k: v for k, v in _L0_gnn_all.items() if k in ('W_lang', 'W_grav', 'W_V', 'W_O', 'gate_logit', 'log_sigma')}
    del _L0_gnn_all
    return {'x': x, 'adj': adj, 'L0_gnn_W_lang': _L0_gnn_in['W_lang'], 'L0_gnn_W_grav': _L0_gnn_in['W_grav'], 'L0_gnn_W_V': _L0_gnn_in['W_V'], 'L0_gnn_W_O': _L0_gnn_in['W_O'], 'L0_gnn_gate_logit': _L0_gnn_in['gate_logit'], 'L0_gnn_log_sigma': _L0_gnn_in['log_sigma']}

def reference(x, adj, L0_gnn_W_lang, L0_gnn_W_grav, L0_gnn_W_V, L0_gnn_W_O, L0_gnn_gate_logit, L0_gnn_log_sigma):
    import jax
    import jax.numpy as jnp

    def _L0_gnn_ref(h, causal_mask, W_lang, W_grav, W_V, W_O, gate_logit, log_sigma):
        import jax, jax.numpy as jnp
        import numpy as np
        EPS = 1e-08

        def _row_stochastic_causal(A, causal_mask):
            A = A * causal_mask
            deg = jnp.maximum(A.sum(axis=-1, keepdims=True), EPS)
            return A / deg
        z_l = jnp.einsum('bnd,ed->bne', h, W_lang)
        z_g = jnp.einsum('bnd,ed->bne', h, W_grav)
        v = jnp.einsum('bnd,ed->bne', h, W_V)
        N = h.shape[-2]
        not_eye = 1.0 - jnp.eye(N, dtype=h.dtype)
        zn = z_l / jnp.maximum(jnp.linalg.norm(z_l, axis=-1, keepdims=True), EPS)
        A_l = jnp.maximum(jnp.einsum('bnd,bmd->bnm', zn, zn), 0.0) * not_eye
        sq = jnp.sum(z_g * z_g, axis=-1, keepdims=True)
        d2 = jnp.maximum(sq + jnp.swapaxes(sq, -1, -2) - 2.0 * jnp.einsum('bnd,bmd->bnm', z_g, z_g), 0.0)
        sigma = jnp.exp(log_sigma)
        A_g = jnp.exp(-d2 / (2.0 * sigma * sigma)) * not_eye
        K_l = _row_stochastic_causal(A_l, causal_mask)
        K_g = _row_stochastic_causal(A_g, causal_mask)
        w_l = jax.nn.sigmoid(gate_logit)
        K = w_l * K_l + (1.0 - w_l) * K_g
        out = jnp.einsum('bnm,bmd->bnd', K, v)
        return jnp.einsum('bnd,ed->bne', out, W_O)
    h = jnp.maximum(_layernorm(x, axis=-1), 0.0)
    x = x + _L0_gnn_ref(h, adj, L0_gnn_W_lang, L0_gnn_W_grav, L0_gnn_W_V, L0_gnn_W_O, L0_gnn_gate_logit, L0_gnn_log_sigma)
    return x

_drawn_inputs = setup_inputs


def setup_inputs(seed=0):
    import zlib

    import numpy as np

    out = dict(_drawn_inputs(seed))
    spreads = {}
    factors = {}
    for name, (base, spread) in spreads.items():
        noise = np.random.default_rng([zlib.crc32(name.encode()), seed]).standard_normal(out[name].shape)
        drawn = base * np.exp(spread * noise) if base else spread * noise
        out[name] = jnp.asarray(drawn.astype(out[name].dtype))
    for name, factor in factors.items():
        out[name] = (out[name] * factor).astype(out[name].dtype)
    return out
```

```python
from contextlib import ExitStack

import numpy as np

import concourse.bass as bass
from concourse import mybir

F32 = mybir.dt.float32
F16 = mybir.dt.float16
BF16 = mybir.dt.bfloat16
I32 = mybir.dt.int32
ALU = mybir.AluOpType
ACT = mybir.ActivationFunctionType
AX = mybir.AxisListType

P = 128
BANK = 512
H_SCALE = 2.0
W_SCALE = 16.0
K_SCALE = 1024.0
LN_EPS = 1e-5
EPS = 1e-8
HI, LO = 0, 1
L, G = 0, 1
PASSES = ((HI, HI), (HI, LO), (LO, HI))


def gnn_kernel(nc, x, adj, w_lang, w_grav, w_v, w_o, gate_logit, log_sigma, out):
    B, N, D = x.shape
    T = N // P
    KC = D // P
    HALF = N // BANK
    HB = BANK // P
    ZT = 2 * KC * HALF
    ROW_AT = [sum(T - r for r in range(i)) for i in range(T + 1)]

    off_pieces = []
    for i in range(T - 1):
        for m in (L, G):
            j = i + 1
            while j < T:
                n = min(HB, T - j)
                off_pieces.append((m, i, j, n))
                j += n
    OFF = len(off_pieces)

    def ends_row(k):
        return k == OFF - 1 or off_pieces[k + 1][1] != off_pieces[k][1]

    raw_pieces = []
    for i in range(1, T):
        for m in (L, G):
            for j in range(0, i, HB):
                raw_pieces.append((m, i, j, min(HB, i - j)))
    RAW = len(raw_pieces)
    DG = 2 * T // HB
    RW = 2 * HALF

    V_LATE = 3

    def order(last):
        early = T - V_LATE if last else T
        seq = [("diag", k) for k in range(DG)] + [("v", k) for k in range(early)] + [("row", k) for k in range(RW)]
        for k in range(OFF):
            seq.append(("off", k))
            if not last and k % 2 == 1 and k // 2 < T:
                seq.append(("h", k // 2))
        return seq + [("v", k) for k in range(early, T)]

    def last_before_rows(last):
        return T - V_LATE - 1 if last else T - 1

    def z_behind(s):
        return [2 * s + 1] if s < T - 1 else [ZT - 1] if s == T else []

    RAW1_AT = 6
    MASK_AT = {5: (0, L), 7: (0, G), 9: (1, L), 11: (1, G)}
    SCALE_AT = {8: 0, 12: 1}
    COMBINE_AT = {13: 0, 15: 1}

    PM = 3
    assert (len(order(False)) + ZT) % PM == 0 and (T + ZT) % PM == 0

    with ExitStack() as ctx:
        def sb(name, shape, dt=F32):
            return ctx.enter_context(nc.sbuf_tensor(name, shape, dt))

        def sem(name):
            return ctx.enter_context(nc.semaphore(name))

        bank = [ctx.enter_context(nc.psum_tensor(f"bank{i}", [P, BANK], F32)) for i in range(8)]
        ring_bank, raw_bank, kt_bank, kv_bank = bank[0:3], bank[3:5], bank[5:7], bank[7]
        w_bank = bank[3:7]

        ident = sb("ident", [P, P])
        ident16 = sb("ident16", [P, P], BF16)
        spread = sb("spread", [P, 2 * T, P], BF16)
        W = [sb(f"W{i}", [P, 2, KC, D], F16) for i in range(3)]
        adjm = sb("adjm", [P, T, N])
        hT = sb("hT", [P, 2, KC, N], F16)
        zT = [sb(f"zT{m}", [P, 2, KC, N], F16) for m in (L, G)]
        v = sb("v", [P, 2, T, D], F16)
        tri = sb("tri", [P, 2, ROW_AT[T] * P])
        mask_l = sb("mask_l", [P, 2, N])
        mask_g = sb("mask_g", [P, 3, N])
        KT = sb("KT", [P, 2, 2, T, P], F16)
        rows = sb("rows", [P, 2, N])
        xr = sb("xr", [P, 2, D])
        stats = sb("stats", [P, T, 6])
        mv = sb("mv", [P, T, 2])
        ln = sb("ln", [P, T, 4])
        half_neg = sb("half_neg", [P, 1])
        ln_eps = sb("ln_eps", [P, 1])
        h_scale = sb("h_scale", [P, 1])
        h_scale_neg = sb("h_scale_neg", [P, 1])
        half_pos = sb("half_pos", [P, T])
        sq = sb("sq", [P, 2, T])
        nrm = sb("nrm", [P, T])
        col = sb("col", [P, 2, T])
        col_part = sb("col_part", [P, P], BF16)
        col_rest = sb("col_rest", [P, 2, 2 * T])
        colT = sb("colT", [P, P], BF16)
        spare = sb("spare", [P, 1])
        part = sb("part", [P, T, 2, 3])
        deg = sb("deg", [P, 2, 2])
        wr = sb("wr", [P, 2, 2])
        wmax = sb("wmax", [P, 3])
        wall = sb("wall", [P, 3])
        wpow = sb("wpow", [P, 3])
        winv = sb("winv", [P, 3])
        wsc = sb("wsc", [P, 3])
        wun = sb("wun", [P, 3])
        gs = sb("gs", [P, 2])
        gexp = sb("gexp", [P, 2])
        gtmp = sb("gtmp", [P, 4])
        wk = sb("wk", [P, 2])
        beta = sb("beta", [P, 1])
        vun = sb("vun", [P, 1])
        XL = 4
        xl = KT[:, :, :, :, :].rearrange("p a q j n -> p (a q j n)").bitcast(F32).rearrange("p (t d) -> p t d", t=XL)
        x0 = v[:, :, :, :].rearrange("p a t d -> p (a t d)").bitcast(F32).rearrange("p (t d) -> p t d", t=T)
        w_raw = [tri[:, L, i * KC * D:(i + 1) * KC * D].rearrange("p (c d) -> p c d", c=KC) for i in range(2)] + \
                [tri[:, G, i * KC * D:(i + 1) * KC * D].rearrange("p (c d) -> p c d", c=KC) for i in range(2)]
        woT = mask_l[:, :, :].rearrange("p a n -> p (a n)").rearrange("p (c d) -> p c d", c=KC)
        wvo = mask_g[:, 0:2, :].rearrange("p a n -> p (a n)").rearrange("p (c d) -> p c d", c=KC)

        w_loaded = [sem(f"w_loaded{i}") for i in range(4)]
        adj_loaded, gs_loaded = sem("adj_loaded"), sem("gs_loaded")
        spread_step = sem("spread_step")
        consts_ready, ident_ready, adj_ready = sem("consts_ready"), sem("ident_ready"), sem("adj_ready")
        wmax_ready, wall_ready, wscale_ready = sem("wmax_ready"), sem("wall_ready"), sem("wscale_ready")
        wt_full, wt_hi, wt_lo = sem("wt_full"), sem("wt_hi"), sem("wt_lo")
        woT_ready, wvo_full, wvo_ready = sem("woT_ready"), sem("wvo_full"), sem("wvo_ready")
        gexp_ready, scal_ready = sem("gexp_ready"), sem("scal_ready")
        x0_loaded = [sem(f"x0_loaded{i}") for i in range(T // 2)]
        xl_loaded = [sem(f"xl_loaded{i}") for i in range(XL)]
        xr_loaded = [sem(f"xr_loaded{i}") for i in range(2)]
        stored = [sem(f"stored{i}") for i in range(2)]
        stats_ready, ln_ready, h_ready = sem("stats_ready"), sem("ln_ready"), sem("h_ready")
        full = {k: sem(f"{k}_full") for k in ("diag", "v", "row", "off", "h", "z")}
        hi_ready = {k: sem(f"{k}_hi") for k in ("v", "h", "z")}
        lo_ready = {k: sem(f"{k}_lo") for k in ("v", "h", "z")}
        diag_copied, row_copied, off_done = sem("diag_copied"), sem("row_copied"), sem("off_done")
        sq_ready, nrm_ready = sem("sq_ready"), sem("nrm_ready")
        colpart_ready, colT_full, colT_ready = sem("colpart_ready"), sem("colT_full"), sem("colT_ready")
        corner_done, exp_ready = sem("corner_done"), sem("exp_ready")
        raw_full, raw_masked = sem("raw_full"), sem("raw_masked")
        wr_ready, lscaled, k_ready = sem("wr_ready"), sem("lscaled"), sem("k_ready")
        kt_full, kt_hi, kt_lo = sem("kt_full"), sem("kt_hi"), sem("kt_lo")
        kv_full, out_ready = sem("kv_full"), sem("out_ready")
        pool_step, vec_step = sem("pool_step"), sem("vec_step")

        COUNT = {"diag": DG, "v": T, "row": RW, "off": OFF, "h": T, "z": ZT}
        FREED = {"diag": diag_copied, "v": lo_ready["v"], "row": row_copied, "off": off_done,
                 "h": lo_ready["h"], "z": lo_ready["z"]}

        def nth(per_batch, b, i):
            return b * per_batch + (i + 1)

        def batch_of(kind, b):
            return b + 1 if kind in ("h", "z") else b

        def ring(last):
            seq = order(last) + ([] if last else [("z", k) for k in range(ZT)])
            where = {}
            for g, piece in enumerate(seq):
                before = seq[g - PM] + (0,) if g >= PM else ("z", ZT - PM + g, -1)
                where[piece] = (ring_bank[g % PM], before)
            return where

        RING = {last: ring(last) for last in (False, True)}
        first = [("h", k) for k in range(T // 2)] + [("z", k) for k in range(KC)] + \
                [("h", k) for k in range(T // 2, T)] + [("z", k) for k in range(KC, ZT)]
        FIRST = {p: (ring_bank[g % PM], first[g - PM] + (-1,) if g >= PM else None) for g, p in enumerate(first)}

        def tri_at(m, i, j, n):
            at = (ROW_AT[i] + j - i) * P
            return tri[:, m, at:at + n * P]

        def masked(m, i):
            return mask_l[:, i % 2, :] if m == L else mask_g[:, i % 3, :]

        def z_tile(k):
            return k // (KC * HALF), k % KC, k // KC % HALF

        def split_target(kind, k, p):
            if kind == "v":
                return v[:, p, k, :]
            if kind == "h":
                return hT[:, p, :, k * P:(k + 1) * P]
            m, e, hf = z_tile(k)
            return zT[m][:, p, e, hf * BANK:(hf + 1) * BANK]

        def split_source(kind, bank_):
            return bank_[:, :].rearrange("p (k n) -> p k n", k=KC) if kind == "h" else bank_[:, :]

        block = ctx.enter_context(nc.Block())

        @block.sync
        def _(sp):
            def load_xl(b, i):
                sp.dma_start(xl[:, i % XL, :], x[b, i * P:(i + 1) * P, :]).then_inc(xl_loaded[i % XL], 16)

            def load_xr(b, i):
                sp.dma_start(xr[:, i % 2, :], x[b, i * P:(i + 1) * P, :]).then_inc(xr_loaded[i % 2], 16)

            def store(b, i):
                sp.wait_ge(out_ready, nth(T, b, i))
                sp.dma_start(out[b, i * P:(i + 1) * P, :], xr[:, i % 2, :]).then_inc(stored[i % 2], 16)

            def load_x0(i):
                sp.dma_start(x0[:, 2 * i:2 * i + 2, :],
                             x[0, 2 * i * P:(2 * i + 2) * P, :].rearrange("(t p) d -> p t d", p=P)).then_inc(x0_loaded[i], 16)

            sources = (w_lang, w_grav, w_o, w_v)
            load_x0(0)
            sp.dma_start(w_raw[0], sources[0].rearrange("(c p) d -> p c d", p=P)).then_inc(w_loaded[0], 16)
            sp.dma_start(gs[:, 0:1], bass.AP(gate_logit.tensor, 0, [[0, P], [1, 1]])).then_inc(gs_loaded, 16)
            sp.dma_start(gs[:, 1:2], bass.AP(log_sigma.tensor, 0, [[0, P], [1, 1]])).then_inc(gs_loaded, 16)
            for i in range(1, T // 2):
                load_x0(i)
            for i in range(1, 4):
                sp.dma_start(w_raw[i], sources[i].rearrange("(c p) d -> p c d", p=P)).then_inc(w_loaded[i], 16)
            sp.dma_start(adjm[:, :, :], adj.rearrange("(t p) m -> p t m", p=P)).then_inc(adj_loaded, 16)
            for i in range(2):
                load_xr(0, i)

            def batch(b, last):
                if not last:
                    for i in range(T):
                        if i < XL:
                            sp.wait_ge(full["diag"], nth(DG, b, 0))
                        else:
                            sp.wait_ge(full["h"], nth(T, b + 1, i - XL))
                        load_xl(b + 1, i)
                for i in range(T):
                    store(b, i)
                    if i + 2 < T or not last:
                        sp.wait_ge(stored[i % 2], 16 * nth(T // 2, b, i // 2))
                        if i + 2 < T:
                            load_xr(b, i + 2)
                        else:
                            load_xr(b + 1, i + 2 - T)

            with sp.Fori(0, B - 1) as b:
                batch(b, False)
            batch(B - 1, True)
            for j in range(2):
                sp.wait_ge(stored[j], 16 * B * T // 2)

        @block.gpsimd
        def _(pool):
            nc.gpsimd.memset(ident16[:, :], 0.0)
            nc.gpsimd.memset(half_neg[:, :], -0.5)
            nc.gpsimd.memset(half_pos[:, :], 0.5)
            nc.gpsimd.memset(ln_eps[:, :], LN_EPS)
            nc.gpsimd.memset(h_scale[:, :], H_SCALE)
            nc.gpsimd.memset(h_scale_neg[:, :], -H_SCALE)
            nc.gpsimd.memset(ident[:, :], 0.0).then_inc(consts_ready, 1)
            pool.wait_ge(consts_ready, 1)
            nc.gpsimd.affine_select(out=ident[:, :], in_=ident[:, :], compare_op=ALU.not_equal, fill=1.0, base=0,
                                    pattern=[[-1, P]], channel_multiplier=1).then_inc(ident_ready, 1)
            nc.gpsimd.affine_select(out=ident16[:, :], in_=ident16[:, :], compare_op=ALU.not_equal, fill=1.0, base=0,
                                    pattern=[[-1, P]], channel_multiplier=1)
            steps = [0]

            def step(ins):
                steps[0] += 1
                ins.then_inc(pool_step, 1)
                return steps[0]

            def layernorm(b, i):
                s = ln[:, i, :]
                pool.wait_ge(stats_ready, nth(T, b, i))
                k = step(nc.gpsimd.tensor_tensor(s[:, 0:1], mv[:, i, 1:2], ln_eps[:, :], ALU.add))
                pool.wait_ge(pool_step, base(b) + k)
                k = step(nc.gpsimd.tensor_tensor(s[:, 0:1], s[:, 0:1], half_neg[:, :], ALU.pow))
                pool.wait_ge(pool_step, base(b) + k)
                nc.gpsimd.tensor_tensor(s[:, 1:2], s[:, 0:1], h_scale[:, :], ALU.mult)
                k = step(nc.gpsimd.tensor_tensor(s[:, 2:3], s[:, 0:1], h_scale_neg[:, :], ALU.mult))
                pool.wait_ge(pool_step, base(b) + k)
                nc.gpsimd.tensor_tensor(s[:, 3:4], mv[:, i, 0:1], s[:, 2:3], ALU.mult).then_inc(ln_ready, 1)

            def base(b):
                return b * (3 * T)

            def all_max(w):
                pool.wait_ge(wmax_ready, w + 1)
                nc.gpsimd.partition_all_reduce(wall[:, w:w + 1], wmax[:, w:w + 1], P,
                                               bass.bass_isa.ReduceOp.max).then_inc(wall_ready, 1)

            for i in range(2):
                layernorm(0, i)
            all_max(0)
            for i in range(2, T):
                layernorm(0, i)
            all_max(1)
            nc.gpsimd.memset(spread[:, :, :], 0.0).then_inc(spread_step, 1)
            for q in range(3):
                pool.wait_ge(spread_step, q + 1)
                nc.gpsimd.affine_select(out=spread[:, :, :], in_=spread[:, :, :], compare_op=ALU.not_equal, fill=1.0,
                                        base=-2 * T * q, pattern=[[-1, 2 * T], [0, P]],
                                        channel_multiplier=1).then_inc(spread_step, 1)
            all_max(2)
            pool.wait_ge(adj_loaded, 16)
            for i in range(T):
                d = adjm[:, i, i * P:(i + 1) * P]
                nc.gpsimd.affine_select(out=d, in_=d, compare_op=ALU.not_equal, fill=0.0, base=0,
                                        pattern=[[-1, P]], channel_multiplier=1).then_inc(adj_ready, 1)

            def batch(b, last):
                pool.wait_ge(sq_ready, nth(1, b, 0))
                nc.gpsimd.tensor_tensor(nrm[:, :], sq[:, L, :], half_pos[:, :], ALU.pow).then_inc(nrm_ready, 1)
                if not last:
                    steps[0] = 0
                    for i in range(T):
                        layernorm(b + 1, i)

            with pool.Fori(0, B - 1) as b:
                batch(b, False)
            batch(B - 1, True)

        @block.scalar
        def _(act):
            def high(kind, b, k, where):
                act.wait_ge(full[kind], nth(COUNT[kind], b, k))
                nc.scalar.activation(split_target(kind, k, HI), split_source(kind, where), ACT.Copy).then_inc(hi_ready[kind], 1)

            def make_h(b, i, t):
                act.wait_ge(ln_ready, nth(T, b, i))
                nc.scalar.activation(t, t, ACT.Relu, bias=ln[:, i, 3:4],
                                     scale=ln[:, i, 1:2]).then_inc(h_ready, 1)

            act.wait_ge(gs_loaded, 32)
            nc.scalar.activation(gexp[:, 0:1], gs[:, 0:1], ACT.Exp, scale=-1.0)
            nc.scalar.activation(gexp[:, 1:2], gs[:, 1:2], ACT.Exp).then_inc(gexp_ready, 1)
            def high_weights(w):
                act.wait_ge(wscale_ready, w + 1)
                for k in range(KC):
                    act.wait_ge(wt_full, w * KC + k + 1)
                    nc.scalar.activation(W[w][:, HI, k, :], w_bank[k][:, :], ACT.Copy, scale=wsc[:, w:w + 1]).then_inc(wt_hi, 1)

            make_h(0, 0, x0[:, 0, :])
            make_h(0, 1, x0[:, 1, :])
            for kind, k in first:
                if (kind, k) == ("h", 2):
                    high_weights(0)
                high(kind, 0, k, FIRST[kind, k][0])
                if kind == "h" and k + 2 < T:
                    make_h(0, k + 2, x0[:, k + 2, :])
                if (kind, k) == ("z", KC):
                    high_weights(1)
                if (kind, k) == ("z", ZT // 2):
                    for c in range(KC):
                        act.wait_ge(wt_full, 2 * KC + c + 1)
                        nc.scalar.activation(woT[:, c, :], w_bank[c][:, :], ACT.Copy).then_inc(woT_ready, 1)
            for k in range(KC):
                act.wait_ge(wvo_full, k + 1)
                nc.scalar.activation(wvo[:, k, :], w_bank[k][:, :], ACT.Copy).then_inc(wvo_ready, 1)
            act.wait_ge(wscale_ready, 3)
            for k in range(KC):
                nc.scalar.activation(W[2][:, HI, k, :], wvo[:, k, :], ACT.Copy, scale=wsc[:, 2:3]).then_inc(wt_hi, 1)

            def batch(b, last):
                where = RING[last]
                for k in range(DG):
                    act.wait_ge(full["diag"], nth(DG, b, k))
                    m, i0 = k * HB // T, k * HB % T
                    for i in range(HB):
                        ins = nc.scalar.activation(tri_at(m, i0 + i, i0 + i, 1), where["diag", k][0][:, i * P:(i + 1) * P], ACT.Copy)
                    ins.then_inc(diag_copied, 1)
                for kind, k in order(last)[DG:]:
                    if kind == "v":
                        if k == last_before_rows(last):
                            act.wait_ge(colT_full, nth(1, b, 0))
                            nc.scalar.activation(colT[:, :], kv_bank[:, 0:P // 2].bitcast(BF16), ACT.Copy).then_inc(colT_ready, 1)
                        high("v", b, k, where["v", k][0])
                    if kind == "row":
                        act.wait_ge(full["row"], nth(RW, b, k))
                        m, hf = k // HALF, k % HALF
                        nc.scalar.activation(rows[:, m, hf * BANK:(hf + 1) * BANK], where["row", k][0][:, :], ACT.Copy).then_inc(row_copied, 1)
                        if k == RW - 1 and not last:
                            make_h(b + 1, 0, xl[:, 0, :])
                    if kind == "h":
                        high("h", b + 1, k, where["h", k][0])
                        if k + 1 < T:
                            make_h(b + 1, k + 1, xl[:, (k + 1) % XL, :])
                    if kind == "off" and ends_row(k):
                        exp_row(b, off_pieces[k][1])
                    if kind == "off" and k in SCALE_AT:
                        scale_language(b, SCALE_AT[k])
                exp_row(b, T - 1)
                for s in range(T + 1):
                    if s < T and not last:
                        high("z", b + 1, 2 * s, where["z", 2 * s][0])
                    for hf in range(HALF if s < T else 0):
                        act.wait_ge(kt_full, nth(T * HALF, b, s * HALF + hf))
                        nc.scalar.activation(KT[:, s % 2, HI, hf * HB:(hf + 1) * HB, :],
                                             kt_bank[hf][:, :].rearrange("p (j n) -> p j n", j=HB), ACT.Copy).then_inc(kt_hi, 1)
                    for k in z_behind(s):
                        if not last:
                            high("z", b + 1, k, where["z", k][0])
                    if s + 2 < T:
                        scale_language(b, s + 2)

            def scale_language(b, i):
                act.wait_ge(wr_ready, nth(T, b, i))
                nc.scalar.activation(masked(L, i), masked(L, i), ACT.Copy, scale=wr[:, i % 2, L:L + 1]).then_inc(lscaled, 1)

            def exp_row(b, i):
                if i < T - 1:
                    act.wait_ge(off_done, nth(OFF, b, max(k for k in range(OFF) if off_pieces[k][1] == i)))
                else:
                    act.wait_ge(corner_done, nth(1, b, 0))
                t = tri_at(G, i, i, T - i)
                nc.scalar.activation(t, t, ACT.Exp, scale=beta[:, 0:1]).then_inc(exp_ready, 1)

            act.wait_ge(scal_ready, 1)
            with act.Fori(0, B - 1) as b:
                batch(b, False)
            batch(B - 1, True)

        @block.vector
        def _(dve):
            steps = [0, 0]

            def link(ins, b=None):
                steps[1 if b is not None else 0] += 1
                ins.then_inc(vec_step, 1)
                if b is None:
                    dve.wait_ge(vec_step, steps[0])
                else:
                    dve.wait_ge(vec_step, b * LINKS + (steps[0] + steps[1]))

            def low(kind, b, k, where):
                dve.wait_ge(hi_ready[kind], nth(COUNT[kind], b, k))
                nc.vector.tensor_tensor(split_target(kind, k, LO), split_source(kind, where), split_target(kind, k, HI),
                                        ALU.subtract).then_inc(lo_ready[kind], 1)

            def statistics(i, b=None):
                if b is None:
                    dve.wait_ge(x0_loaded[i // 2], 16)
                else:
                    dve.wait_ge(xl_loaded[i % XL], 16 * nth(T // XL, b, i // XL))
                link(nc.vector.bn_stats(stats[:, i, :], x0[:, i, :] if b is None else xl[:, i % XL, :]), b)
                nc.vector.memset(spare[:, :], 0.0)
                nc.vector.bn_aggr(mv[:, i, :], stats[:, i, :]).then_inc(stats_ready, 1)

            def scale_of(w):
                dve.wait_ge(wall_ready, w + 1)
                c = slice(w, w + 1)
                link(nc.vector.tensor_scalar_max(wpow[:, c], wall[:, c], 1e-30))
                link(nc.vector.tensor_single_scalar(wpow[:, c].bitcast(I32), wpow[:, c].bitcast(I32), 0x7F800000, ALU.bitwise_and))
                link(nc.vector.tensor_scalar(winv[:, c].bitcast(I32), wpow[:, c].bitcast(I32), -1.0, float(0x7F000000), ALU.mult, ALU.add))
                nc.vector.tensor_scalar_mul(wun[:, c], wpow[:, c], 1.0 / (W_SCALE * H_SCALE))
                nc.vector.tensor_scalar_mul(wsc[:, c], winv[:, c], W_SCALE).then_inc(wscale_ready, 1)

            def low_weights(w, k, src):
                dve.wait_ge(wt_hi, w * KC + k + 1)
                nc.vector.scalar_tensor_tensor(W[w][:, LO, k, :], src, wsc[:, w:w + 1], W[w][:, HI, k, :], ALU.mult, ALU.subtract).then_inc(wt_lo, 1)

            def largest(w, src):
                nc.vector.tensor_reduce(wmax[:, w:w + 1], src, AX.XY, ALU.max, apply_absolute_value=True).then_inc(wmax_ready, 1)

            def split_weights(w):
                for k in range(KC):
                    low_weights(w, k, w_bank[k][:, :])

            nc.vector.memset(col_part[:, :], 0.0)
            for i in range(2):
                statistics(i)
            dve.wait_ge(w_loaded[0], 16)
            largest(0, w_raw[0])
            for i in range(2, 4):
                statistics(i)
            scale_of(0)
            for kind, k in first:
                if (kind, k) == ("h", 2):
                    split_weights(0)
                low(kind, 0, k, FIRST[kind, k][0])
                if kind == "h" and k + 4 < T:
                    statistics(k + 4)
                if (kind, k) == ("h", T // 2 - 1):
                    dve.wait_ge(w_loaded[1], 16)
                    largest(1, w_raw[1])
                if (kind, k) == ("z", KC - 1):
                    scale_of(1)
                if (kind, k) == ("z", KC):
                    split_weights(1)
            dve.wait_ge(wvo_ready, KC)
            largest(2, wvo)
            dve.wait_ge(gexp_ready, 1)
            link(nc.vector.tensor_scalar_add(gtmp[:, 0:1], gexp[:, 0:1], 1.0))
            link(nc.vector.reciprocal(gtmp[:, 1:2], gtmp[:, 0:1]))
            link(nc.vector.tensor_scalar_mul(wk[:, L:L + 1], gtmp[:, 1:2], K_SCALE))
            link(nc.vector.tensor_scalar(wk[:, G:G + 1], wk[:, L:L + 1], -1.0, K_SCALE, ALU.mult, ALU.add))
            link(nc.vector.tensor_tensor(gtmp[:, 2:3], gexp[:, 1:2], gexp[:, 1:2], ALU.mult))
            link(nc.vector.reciprocal(gtmp[:, 3:4], gtmp[:, 2:3]))
            nc.vector.tensor_scalar(beta[:, :], gtmp[:, 3:4], wun[:, G:G + 1], wun[:, G:G + 1], ALU.mult, ALU.mult).then_inc(scal_ready, 1)
            scale_of(2)
            for k in range(KC):
                low_weights(2, k, wvo[:, k, :])
            link(nc.vector.tensor_scalar_mul(vun[:, :], wun[:, 2:3], 1.0 / K_SCALE))
            dve.wait_ge(adj_ready, T)
            link(nc.vector.memset(part[:, :, :, :], 0.0))

            def mask(b, i, m):
                scalar, op = ((0.0, ALU.max), (1.0, ALU.min))[m]
                for piece, (pm, pi, j, n) in enumerate(raw_pieces):
                    if (pm, pi) == (m, i):
                        dve.wait_ge(raw_full, nth(RAW, b, piece))
                        nc.vector.scalar_tensor_tensor(masked(m, i)[:, j * P:(j + n) * P], raw_bank[piece % 2][:, 0:n * P], scalar,
                                                       adjm[:, i, j * P:(j + n) * P], op, ALU.mult,
                                                       accum_out=part[:, i, m, j // HB:j // HB + 1]).then_inc(raw_masked, 1)
                if m == G:
                    dve.wait_ge(exp_ready, nth(T, b, i))
                ins = nc.vector.scalar_tensor_tensor(masked(m, i)[:, i * P:N], tri_at(m, i, i, T - i), scalar,
                                                     adjm[:, i, i * P:N], op, ALU.mult, accum_out=part[:, i, m, 2:3])
                if m == G:
                    r = i % 2
                    link(ins, b)
                    link(nc.vector.reduce_sum(deg[:, r, :], part[:, i, :, :], AX.X), b)
                    link(nc.vector.tensor_scalar_max(deg[:, r, :], deg[:, r, :], EPS), b)
                    link(nc.vector.reciprocal(deg[:, r, :], deg[:, r, :]), b)
                    nc.vector.tensor_tensor(wr[:, r, :], deg[:, r, :], wk[:, :], ALU.mult).then_inc(wr_ready, 1)

            def combine(b, i):
                dve.wait_ge(lscaled, nth(T, b, i))
                nc.vector.scalar_tensor_tensor(masked(G, i), masked(G, i), wr[:, i % 2, G:G + 1], masked(L, i),
                                               ALU.mult, ALU.add).then_inc(k_ready, 1)

            def batch(b, last):
                where = RING[last]
                steps[1] = 0
                for m in (L, G):
                    for i in range(T):
                        if i % HB == 0:
                            dve.wait_ge(diag_copied, nth(DG, b, (m * T + i) // HB))
                        ins = nc.vector.scalar_tensor_tensor(masked(m, 0)[:, i * P:(i + 1) * P], tri_at(m, i, i, 1), 1.0, ident[:, :], ALU.mult, ALU.mult,
                                                             accum_out=sq[:, m, i:i + 1])
                    if m == L:
                        ins.then_inc(sq_ready, 1)
                low("v", b, 0, where["v", 0][0])
                dve.wait_ge(nrm_ready, nth(1, b, 0))
                link(nc.vector.tensor_scalar(nrm[:, :], nrm[:, :], wun[:, L:L + 1], EPS, ALU.mult, ALU.max), b)
                link(nc.vector.reciprocal(nrm[:, :], nrm[:, :]), b)
                nc.vector.tensor_scalar(col[:, L, :], nrm[:, :], wun[:, L:L + 1], None, ALU.mult)
                link(nc.vector.tensor_scalar_mul(col[:, G, :], sq[:, G, :], 0.5), b)
                low("v", b, 1, where["v", 1][0])
                C = 2 * T
                rest = col[:, :, :].rearrange("p m t -> p (m t)")
                for q in range(2):
                    link(nc.vector.tensor_copy(col_part[:, q * C:(q + 1) * C], rest), b)
                    link(nc.vector.tensor_tensor(col_rest[:, q, :], rest, col_part[:, q * C:(q + 1) * C], ALU.subtract), b)
                    rest = col_rest[:, q, :]
                nc.vector.tensor_copy(col_part[:, 2 * C:3 * C], rest).then_inc(colpart_ready, 1)
                low("v", b, 2, where["v", 2][0])
                if not last:
                    statistics(0, b)
                    statistics(1, b)

                def finish(m, i, j, n, src):
                    op = ALU.mult if m == L else ALU.subtract
                    return nc.vector.scalar_tensor_tensor(tri_at(m, i, j, n), src, col[:, m, i:i + 1], rows[:, m, j * P:(j + n) * P], op, op)

                for kind, k in order(last)[DG + 3:]:
                    if kind == "v":
                        low("v", b, k, where["v", k][0])
                    if kind == "row" and k == RW - 1:
                        dve.wait_ge(row_copied, nth(RW, b, RW - 1))
                    if kind == "off":
                        m, i, j, n = off_pieces[k]
                        if j == i + 1:
                            finish(m, i, i, 1, tri_at(m, i, i, 1))
                        dve.wait_ge(full["off"], nth(OFF, b, k))
                        ins = finish(m, i, j, n, where["off", k][0][:, 0:n * P])
                        ins.then_inc(off_done, 1)
                        if k in MASK_AT:
                            mask(b, *MASK_AT[k])
                        if k in COMBINE_AT:
                            combine(b, COMBINE_AT[k])
                    if kind == "h":
                        low("h", b + 1, k, where["h", k][0])
                        if k + 2 < T:
                            statistics(k + 2, b)
                finish(L, T - 1, T - 1, 1, tri_at(L, T - 1, T - 1, 1))
                finish(G, T - 1, T - 1, 1, tri_at(G, T - 1, T - 1, 1)).then_inc(corner_done, 1)
                dve.wait_ge(corner_done, nth(1, b, 0))
                for s in range(T + 1):
                    if s < T:
                        if not last:
                            low("z", b + 1, 2 * s, where["z", 2 * s][0])
                        if s + 2 < T:
                            mask(b, s + 2, L)
                        for hf in range(HALF):
                            dve.wait_ge(kt_hi, nth(T * HALF, b, s * HALF + hf))
                            nc.vector.tensor_tensor(KT[:, s % 2, LO, hf * HB:(hf + 1) * HB, :],
                                                    kt_bank[hf][:, :].rearrange("p (j n) -> p j n", j=HB),
                                                    KT[:, s % 2, HI, hf * HB:(hf + 1) * HB, :], ALU.subtract).then_inc(kt_lo, 1)
                    for k in z_behind(s):
                        if not last:
                            low("z", b + 1, k, where["z", k][0])
                    if s + 2 < T and not last:
                        mask(b, s + 2, G)
                        combine(b, s + 2)
                    if s > 0:
                        i = s - 1
                        dve.wait_ge(kv_full, nth(T, b, i))
                        dve.wait_ge(xr_loaded[i % 2], 16 * nth(T // 2, b, i // 2))
                        nc.vector.scalar_tensor_tensor(xr[:, i % 2, :], kv_bank[:, :], vun[:, 0:1], xr[:, i % 2, :],
                                                       ALU.mult, ALU.add).then_inc(out_ready, 1)
                    if s + 2 < T and last:
                        mask(b, s + 2, G)
                        combine(b, s + 2)

            LINKS = T + 3 + 4 + 4 * T
            with dve.Fori(0, B - 1) as b:
                batch(b, False)
            assert steps[1] == LINKS
            batch(B - 1, True)

        @block.tensor
        def _(pe):
            def transpose(dst, src):
                return nc.tensor.transpose(dst, src, ident[:, :])

            def free_of(before, b):
                kind, k, back = before
                pe.wait_ge(FREED[kind], nth(COUNT[kind], batch_of(kind, b) + back, k))

            def product(dst, pairs):
                n = len(pairs) * len(PASSES)
                at = 0
                for lhs, rhs in pairs:
                    for pl, pr in PASSES:
                        last = nc.tensor.matmul(dst, lhs(pl), rhs(pr), start=at == 0, stop=at == n - 1)
                        at += 1
                return last

            def h_piece(b, k, where, src):
                pe.wait_ge(h_ready, nth(T, b, k))
                for c in range(KC):
                    last = transpose(where[:, c * P:(c + 1) * P], src[:, c * P:(c + 1) * P])
                last.then_inc(full["h"], 1)

            def z_piece(b, k, where):
                m, e, hf = z_tile(k)
                last = product(where[:, :], [(lambda p, c=c: W[m][:, p, c, e * P:(e + 1) * P],
                                              lambda p, c=c: hT[:, p, c, hf * BANK:(hf + 1) * BANK]) for c in range(KC)])
                last.then_inc(full["z"], 1)

            def v_piece(b, k, where):
                last = product(where[:, :], [(lambda p, c=c: hT[:, p, c, k * P:(k + 1) * P],
                                              lambda p, c=c: W[2][:, p, c, :]) for c in range(KC)])
                last.then_inc(full["v"], 1)

            def gram(m, i, j, n, dst):
                return product(dst, [(lambda p, c=c: zT[m][:, p, c, i * P:(i + 1) * P],
                                      lambda p, c=c: zT[m][:, p, c, j * P:(j + n) * P]) for c in range(KC)])

            def transpose_weights(w):
                pe.wait_ge(w_loaded[w], 16)
                for k in range(KC):
                    if w:
                        pe.wait_ge(wt_lo, (w - 1) * KC + k + 1)
                    for c in range(KC):
                        last = transpose(w_bank[k][:, c * P:(c + 1) * P], w_raw[w][:, c, k * P:(k + 1) * P])
                    last.then_inc(wt_full, 1)

            pe.wait_ge(ident_ready, 1)
            transpose_weights(0)
            for kind, k in first:
                if (kind, k) == ("z", 0):
                    pe.wait_ge(wt_lo, KC)
                if (kind, k) == ("z", KC):
                    transpose_weights(1)
                if (kind, k) == ("z", ZT // 2):
                    transpose_weights(2)
                where, before = FIRST[kind, k]
                if before:
                    free_of(before, 0)
                if kind == "h":
                    h_piece(0, k, where, x0[:, k, :])
                else:
                    if k % KC == 0:
                        pe.wait_ge(lo_ready["h"], T // 2 if k == 0 else T)
                    z_piece(0, k, where)
            pe.wait_ge(w_loaded[3], 16)
            pe.wait_ge(woT_ready, KC)
            for k in range(KC):
                for f in range(KC):
                    last = nc.tensor.matmul(w_bank[k][:, :], w_raw[3][:, f, k * P:(k + 1) * P], woT[:, f, :],
                                            start=f == 0, stop=f == KC - 1)
                last.then_inc(wvo_full, 1)
            pe.wait_ge(spread_step, 4)

            def batch(b, last_batch):
                where = RING[last_batch]

                def take(kind, k):
                    bank_, before = where[kind, k]
                    free_of(before, b)
                    return bank_

                def raws(m, i):
                    for piece, (pm, pi, j, n) in enumerate(raw_pieces):
                        if (pm, pi) == (m, i):
                            if piece >= 2:
                                pe.wait_ge(raw_masked, nth(RAW, b, piece - 2))
                            if m == L:
                                pe.wait_ge(off_done, nth(OFF, b, 0 if i == 1 else OFF - 1))
                            if m == G:
                                pe.wait_ge(exp_ready, nth(T, b, j + n - 1))
                            for q in range(n):
                                last = transpose(raw_bank[piece % 2][:, q * P:(q + 1) * P], tri_at(m, j + q, i, 1))
                            last.then_inc(raw_full, 1)

                for kind, k in order(last_batch):
                    if (kind, k) == ("v", last_before_rows(last_batch)):
                        pe.wait_ge(colpart_ready, nth(1, b, 0))
                        nc.tensor.transpose(kv_bank[:, 0:P // 2].bitcast(BF16), col_part[:, :], ident16[:, :]).then_inc(colT_full, 1)
                    if kind == "row" and k == 0:
                        pe.wait_ge(colT_ready, nth(1, b, 0))
                    bank_ = take(kind, k)
                    if kind == "diag":
                        m, i0 = k * HB // T, k * HB % T
                        if i0 == 0:
                            pe.wait_ge(lo_ready["z"], nth(ZT, b, (m + 1) * ZT // 2 - 1))
                        for i in range(HB):
                            last = gram(m, i0 + i, i0 + i, 1, bank_[:, i * P:(i + 1) * P])
                        last.then_inc(full["diag"], 1)
                    if kind == "v":
                        if k == 0:
                            pe.wait_ge(wt_lo, 3 * KC)
                        v_piece(b, k, bank_)
                    if kind == "row":
                        for c in range(HB):
                            last = nc.tensor.matmul(bank_[:, c * P:(c + 1) * P], spread[:, k * HB + c, :], colT[:, :],
                                                    start=True, stop=True)
                        last.then_inc(full["row"], 1)
                    if kind == "off":
                        m, i, j, n = off_pieces[k]
                        gram(m, i, j, n, bank_[:, 0:n * P]).then_inc(full["off"], 1)
                        if k == RAW1_AT:
                            raws(L, 1)
                            raws(G, 1)
                    if kind == "h":
                        h_piece(b + 1, k, bank_, xl[:, k % XL, :])

                def z_next(k):
                    if not last_batch:
                        if k == 0:
                            pe.wait_ge(lo_ready["h"], nth(T, b + 1, T - 1))
                        z_piece(b + 1, k, take("z", k))

                def aggregate(i):
                    if i > 0:
                        pe.wait_ge(out_ready, nth(T, b, i - 1))
                    else:
                        pe.wait_ge(lo_ready["v"], nth(T, b, T - 1))
                    at = 0
                    for j in range(T):
                        if j % HB == 0:
                            pe.wait_ge(kt_lo, nth(T * HALF, b, i * HALF + j // HB))
                        for pl, pr in PASSES:
                            last = nc.tensor.matmul(kv_bank[:, :], KT[:, i % 2, pl, j, :], v[:, pr, j, :], start=at == 0,
                                                    stop=at == T * len(PASSES) - 1)
                            at += 1
                    last.then_inc(kv_full, 1)

                for s in range(T + 1):
                    if s < T:
                        z_next(2 * s)
                        if s + 2 < T:
                            raws(L, s + 2)
                        pe.wait_ge(k_ready, nth(T, b, s))
                        for hf in range(HALF):
                            if s > 0:
                                pe.wait_ge(kt_lo, nth(T * HALF, b, (s - 1) * HALF + hf))
                            for q in range(HB):
                                j = hf * HB + q
                                last = transpose(kt_bank[hf][:, q * P:(q + 1) * P], masked(G, s)[:, j * P:(j + 1) * P])
                            last.then_inc(kt_full, 1)
                    for k in z_behind(s):
                        z_next(k)
                    if s + 2 < T and not last_batch:
                        raws(G, s + 2)
                    if s > 0:
                        aggregate(s - 1)
                    if s + 2 < T and last_batch:
                        raws(G, s + 2)

            with pe.Fori(0, B - 1) as b:
                batch(b, False)
            batch(B - 1, True)


_INS = ["x", "adj", "L0_gnn_W_lang", "L0_gnn_W_grav", "L0_gnn_W_V", "L0_gnn_W_O", "L0_gnn_gate_logit", "L0_gnn_log_sigma"]


def kernel(**inputs):
    import concourse.bacc as bacc
    from concourse.bass_utils import run_bass_kernel_spmd

    nc = bacc.Bacc("TRN2", target_bir_lowering=False, num_devices=1)
    arrays, args = {}, []
    for name in _INS:
        a = np.ascontiguousarray(inputs[name])
        if a.ndim == 0:
            a = a.reshape(1)
        arrays[f"in_{name}_dram"] = a
        args.append(nc.dram_tensor(f"in_{name}_dram", a.shape, mybir.dt.from_np(a.dtype), kind="ExternalInput").ap())
    x = inputs["x"]
    args.append(nc.dram_tensor("out_0_dram", x.shape, F32, kind="ExternalOutput").ap())
    gnn_kernel(nc, *args)
    r = run_bass_kernel_spmd(nc, [arrays], core_ids=[0])
    return r.results[0]["out_0_dram"]
```

```python
from contextlib import ExitStack

import numpy as np

import concourse.bass as bass
from concourse import mybir

F32 = mybir.dt.float32
F16 = mybir.dt.float16
BF16 = mybir.dt.bfloat16
I32 = mybir.dt.int32
ALU = mybir.AluOpType
ACT = mybir.ActivationFunctionType
AX = mybir.AxisListType

P = 128
BANK = 512
Q = 32
NQ = P // Q
H_SCALE = 2.0
W_SCALE = 16.0
K_SCALE = 1024.0
LN_EPS = 1e-5
EPS = 1e-8
HI, LO = 0, 1
L, G = 0, 1
PASSES = ((HI, HI), (HI, LO), (LO, HI))


def gnn_kernel(nc, x, adj, w_lang, w_grav, w_v, w_o, gate_logit, log_sigma, out):
    B, N, D = x.shape
    T = N // P
    KC = D // P
    HALF = N // BANK
    HB = BANK // P
    ZT = 2 * KC * HALF
    ROW_AT = [sum(T - r for r in range(i)) for i in range(T + 1)]

    off_pieces = []
    for i in range(T - 1):
        for m in (L, G):
            j = i + 1
            while j < T:
                n = min(HB, T - j)
                off_pieces.append((m, i, j, n))
                j += n
    OFF = len(off_pieces)

    def ends_row(k):
        return k == OFF - 1 or off_pieces[k + 1][1] != off_pieces[k][1]

    raw_pieces = []
    for i in range(1, T):
        for m in (L, G):
            for j in range(0, i, HB):
                raw_pieces.append((m, i, j, min(HB, i - j)))
    RAW = len(raw_pieces)
    DG = 2 * T // HB
    RW = 2 * HALF

    V_LATE = 4

    def order(last):
        early = T - V_LATE if last else T
        seq = [("diag", k) for k in range(DG)] + [("v", k) for k in range(early)] + [("row", k) for k in range(RW)]
        for k in range(OFF):
            seq.append(("off", k))
            if not last and k % 2 == 1 and k // 2 < T:
                seq.append(("h", k // 2))
        return seq + [("v", k) for k in range(early, T)]

    def last_before_rows(last):
        return T - V_LATE - 1 if last else T - 1

    def rows_ahead(last):
        return 3 if last else 2

    def late_v(last):
        return {T - V_LATE: L, T - V_LATE + 1: G} if last else {}

    def z_behind(s):
        return [2 * s + 1] if s < T - 1 else [ZT - 1] if s == T else []

    RAW1_AT = 8
    MASK_AT = {5: (0, L), 7: (0, G), 9: (1, L), 11: (1, G)}
    SCALE_AT = {8: 0, 12: 1}
    COMBINE_AT = {13: 0}
    SPLIT0_AT = 14

    PM = 4
    assert HALF == 2 and ZT == 2 * T and T % HB == 0 and RAW1_AT < OFF
    assert (len(order(False)) + ZT) % PM == 0 and (T + ZT) % PM == 0

    with ExitStack() as ctx:
        def sb(name, shape, dt=F32):
            return ctx.enter_context(nc.sbuf_tensor(name, shape, dt))

        def sem(name):
            return ctx.enter_context(nc.semaphore(name))

        bank = [ctx.enter_context(nc.psum_tensor(f"bank{i}", [P, BANK], F32)) for i in range(8)]
        ring_bank, raw_bank, kv_bank = bank[0:PM], bank[PM:PM + 3], bank[PM + 3]
        w_bank = bank[PM:PM + KC]
        colT_bank = kv_bank

        ident = sb("ident", [P, P])
        ident16 = sb("ident16", [P, P], BF16)
        spread = sb("spread", [P, 2 * T, P], BF16)
        W = [sb(f"W{i}", [P, 2, KC, D], F16) for i in range(3)]
        adjm = sb("adjm", [P, T, N])
        hT = sb("hT", [P, 2, KC, N], F16)
        zT = [sb(f"zT{m}", [P, 2, KC, N], F16) for m in (L, G)]
        v = sb("v", [P, 2, T, D], F16)
        tri = sb("tri", [P, 2, ROW_AT[T] * P])
        mask_l = sb("mask_l", [P, 2, N])
        mask_g = sb("mask_g", [P, 3, N])
        kn = sb("kn", [P, NQ, Q, 2, T], F16)
        KT = sb("KT", [P, 2, P, 2, T], F16)
        rows = sb("rows", [P, 2, N])
        xr = sb("xr", [P, 2, D])
        stats = sb("stats", [P, T, 6])
        mv = sb("mv", [P, T, 2])
        ln = sb("ln", [P, T, 4])
        half_neg = sb("half_neg", [P, 1])
        ln_eps = sb("ln_eps", [P, 1])
        h_scale = sb("h_scale", [P, 1])
        h_scale_neg = sb("h_scale_neg", [P, 1])
        half_pos = sb("half_pos", [P, T])
        sq = sb("sq", [P, 2, T])
        nrm = sb("nrm", [P, T])
        col = sb("col", [P, 2, T])
        col_part = sb("col_part", [P, P], BF16)
        col_rest = sb("col_rest", [P, 2, 2 * T])
        colT = sb("colT", [P, P], BF16)
        spare = sb("spare", [P, 1])
        part = sb("part", [P, T, 2, 3])
        deg = sb("deg", [P, 2, 2])
        wr = sb("wr", [P, 2, 2])
        wmax = sb("wmax", [P, 3])
        wall = sb("wall", [P, 3])
        wpow = sb("wpow", [P, 3])
        winv = sb("winv", [P, 3])
        wsc = sb("wsc", [P, 3])
        wun = sb("wun", [P, 3])
        gs = sb("gs", [P, 2])
        gexp = sb("gexp", [P, 2])
        gtmp = sb("gtmp", [P, 4])
        wk = sb("wk", [P, 2])
        beta = sb("beta", [P, 1])
        vun = sb("vun", [P, 1])
        XL = 4
        xl = KT[:, :, :, :, :].rearrange("p a n q j -> p (a n q j)").bitcast(F32).rearrange("p (t d) -> p t d", t=XL)
        k_squares = nc.dram_tensor("k_squares", [2, P * NQ * Q * 2 * T], F16, kind="Internal").ap()
        x0 = v[:, :, :, :].rearrange("p a t d -> p (a t d)").bitcast(F32).rearrange("p (t d) -> p t d", t=T)
        w_raw = [tri[:, L, i * KC * D:(i + 1) * KC * D].rearrange("p (c d) -> p c d", c=KC) for i in range(2)] + \
                [tri[:, G, i * KC * D:(i + 1) * KC * D].rearrange("p (c d) -> p c d", c=KC) for i in range(2)]
        woT = mask_l[:, :, :].rearrange("p a n -> p (a n)").rearrange("p (c d) -> p c d", c=KC)
        wvo = mask_g[:, 0:2, :].rearrange("p a n -> p (a n)").rearrange("p (c d) -> p c d", c=KC)

        w_loaded = [sem(f"w_loaded{i}") for i in range(4)]
        adj_loaded, gs_loaded = sem("adj_loaded"), sem("gs_loaded")
        spread_step = sem("spread_step")
        consts_ready, ident_ready, adj_ready = sem("consts_ready"), sem("ident_ready"), sem("adj_ready")
        wmax_ready, wall_ready, wscale_ready = sem("wmax_ready"), sem("wall_ready"), sem("wscale_ready")
        wt_full, wt_hi, wt_lo = sem("wt_full"), sem("wt_hi"), sem("wt_lo")
        woT_ready, wvo_full, wvo_ready = sem("woT_ready"), sem("wvo_full"), sem("wvo_ready")
        gexp_ready, scal_ready = sem("gexp_ready"), sem("scal_ready")
        x0_loaded = [sem(f"x0_loaded{i}") for i in range(T // 2)]
        xl_loaded = [sem(f"xl_loaded{i}") for i in range(XL)]
        xr_loaded = [sem(f"xr_loaded{i}") for i in range(2)]
        stored = [sem(f"stored{i}") for i in range(2)]
        stats_ready, ln_ready, h_ready = sem("stats_ready"), sem("ln_ready"), sem("h_ready")
        full = {k: sem(f"{k}_full") for k in ("diag", "v", "row", "off", "h", "z")}
        hi_ready = {k: sem(f"{k}_hi") for k in ("v", "h", "z")}
        lo_ready = {k: sem(f"{k}_lo") for k in ("v", "h", "z")}
        diag_copied, row_copied, off_done = sem("diag_copied"), sem("row_copied"), sem("off_done")
        sq_ready, nrm_ready = sem("sq_ready"), sem("nrm_ready")
        colpart_ready, colT_full, colT_ready = sem("colpart_ready"), sem("colT_full"), sem("colT_ready")
        corner_done, exp_ready = sem("corner_done"), sem("exp_ready")
        raw_full, raw_masked = sem("raw_full"), sem("raw_masked")
        wr_ready, lscaled, k_combined, k_ready = sem("wr_ready"), sem("lscaled"), sem("k_combined"), sem("k_ready")
        k_hi, k_split, k_written, half_free = sem("k_hi"), sem("k_split"), sem("k_written"), sem("half_free")
        kt_ready = [sem(f"kt_ready{i}") for i in range(2)]
        kv_full, out_ready = sem("kv_full"), sem("out_ready")
        pool_step, vec_step = sem("pool_step"), sem("vec_step")

        COUNT = {"diag": DG, "v": T, "row": RW, "off": OFF, "h": T, "z": ZT}
        FREED = {"diag": diag_copied, "v": lo_ready["v"], "row": row_copied, "off": off_done,
                 "h": lo_ready["h"], "z": lo_ready["z"]}

        def nth(per_batch, b, i):
            return b * per_batch + (i + 1)

        def batch_of(kind, b):
            return b + 1 if kind in ("h", "z") else b

        def ring(last):
            seq = order(last) + ([] if last else [("z", k) for k in range(ZT)])
            where = {}
            for g, piece in enumerate(seq):
                before = seq[g - PM] + (0,) if g >= PM else ("z", ZT - PM + g, -1)
                where[piece] = (ring_bank[g % PM], before)
            return where

        RING = {last: ring(last) for last in (False, True)}
        first = [("h", k) for k in range(T // 2)] + [("z", k) for k in range(KC)] + \
                [("h", k) for k in range(T // 2, T)] + [("z", k) for k in range(KC, ZT)]
        FIRST = {p: (ring_bank[g % PM], first[g - PM] + (-1,) if g >= PM else None) for g, p in enumerate(first)}

        RAW4 = min(q for q, piece in enumerate(raw_pieces) if piece[1] == 4)

        def raw_at(q, last):
            if last and q >= RAW4:
                turn = q - RAW4
                return (ring_bank + raw_bank[0:2])[turn % (PM + 2)], None if turn < PM else RAW4 - 1 if turn < PM + 2 else q - PM - 2
            n = 2 if last else 3
            return raw_bank[q % n], q - n if q >= n else None

        def product_bank(i, last):
            return raw_bank[2] if last and i % 2 == 1 else kv_bank

        def tri_at(m, i, j, n):
            at = (ROW_AT[i] + j - i) * P
            return tri[:, m, at:at + n * P]

        def masked(m, i):
            return mask_l[:, i % 2, :] if m == L else mask_g[:, i % 3, :]

        def squares(i):
            return masked(G, i).rearrange("p (b n j) -> p b n j", b=NQ, n=Q)

        def z_tile(k):
            return k // (KC * HALF), k % KC, k // KC % HALF

        def split_target(kind, k, p):
            if kind == "v":
                return v[:, p, k, :]
            if kind == "h":
                return hT[:, p, :, k * P:(k + 1) * P]
            m, e, hf = z_tile(k)
            return zT[m][:, p, e, hf * BANK:(hf + 1) * BANK]

        def split_source(kind, bank_):
            return bank_[:, :].rearrange("p (k n) -> p k n", k=KC) if kind == "h" else bank_[:, :]

        block = ctx.enter_context(nc.Block())

        @block.sync
        def _(sp):
            def load_xl(b, i):
                sp.dma_start(xl[:, i % XL, :], x[b, i * P:(i + 1) * P, :]).then_inc(xl_loaded[i % XL], 16)

            def load_xr(b, i):
                sp.dma_start(xr[:, i % 2, :], x[b, i * P:(i + 1) * P, :]).then_inc(xr_loaded[i % 2], 16)

            def store(b, i):
                sp.wait_ge(out_ready, nth(T, b, i))
                sp.dma_start(out[b, i * P:(i + 1) * P, :], xr[:, i % 2, :]).then_inc(stored[i % 2], 16)

            def load_x0(i):
                sp.dma_start(x0[:, 2 * i:2 * i + 2, :],
                             x[0, 2 * i * P:(2 * i + 2) * P, :].rearrange("(t p) d -> p t d", p=P)).then_inc(x0_loaded[i], 16)

            sources = (w_lang, w_grav, w_o, w_v)
            load_x0(0)
            sp.dma_start(w_raw[0], sources[0].rearrange("(c p) d -> p c d", p=P)).then_inc(w_loaded[0], 16)
            sp.dma_start(gs[:, 0:1], bass.AP(gate_logit.tensor, 0, [[0, P], [1, 1]])).then_inc(gs_loaded, 16)
            sp.dma_start(gs[:, 1:2], bass.AP(log_sigma.tensor, 0, [[0, P], [1, 1]])).then_inc(gs_loaded, 16)
            for i in range(1, T // 2):
                load_x0(i)
            for i in range(1, 4):
                sp.dma_start(w_raw[i], sources[i].rearrange("(c p) d -> p c d", p=P)).then_inc(w_loaded[i], 16)
            sp.dma_start(adjm[:, :, :], adj.rearrange("(t p) m -> p t m", p=P)).then_inc(adj_loaded, 16)
            for i in range(2):
                load_xr(0, i)

            def batch(b, last):
                if not last:
                    for i in range(T):
                        if i < XL:
                            sp.wait_ge(full["diag"], nth(DG, b, 0))
                        else:
                            sp.wait_ge(full["h"], nth(T, b + 1, i - XL))
                        load_xl(b + 1, i)
                    sp.wait_ge(full["h"], nth(T, b + 1, T - 1))
                for s in range(T + 2):
                    if s < T:
                        if s > 1:
                            sp.wait_ge(kt_ready[s % 2], 16 * NQ * nth(T // 2, b, s // 2 - 1))
                            sp.sem_inc(half_free, 1)
                        sp.wait_ge(k_split, nth(T, b, s))
                        sp.dma_start(k_squares[s % 2].rearrange("(p f) -> p f", p=P),
                                     kn[:, :, :, :, :].rearrange("p c n q j -> p (c n q j)")).then_inc(k_written, 16)
                    if s > 1:
                        store(b, s - 2)
                    if s < T:
                        sp.wait_ge(k_written, 16 * nth(T, b, s))
                        for c in range(NQ):
                            sp.dma_start(KT[c * Q:(c + 1) * Q, s % 2, :, :, :].rearrange("m (a n) q j -> m a (n q j)", a=NQ),
                                         k_squares[s % 2].rearrange("(a m c f) -> c m a f", a=NQ, m=Q, c=NQ)[c]).then_inc(kt_ready[s % 2], 16)
                    if s > 1:
                        i = s - 2
                        if i + 2 < T or not last:
                            sp.wait_ge(stored[i % 2], 16 * nth(T // 2, b, i // 2))
                            if i + 2 < T:
                                load_xr(b, i + 2)
                            else:
                                load_xr(b + 1, i + 2 - T)

            with sp.Fori(0, B - 1) as b:
                batch(b, False)
            batch(B - 1, True)
            for j in range(2):
                sp.wait_ge(stored[j], 16 * B * T // 2)

        @block.gpsimd
        def _(pool):
            nc.gpsimd.memset(ident16[:, :], 0.0)
            nc.gpsimd.memset(half_neg[:, :], -0.5)
            nc.gpsimd.memset(half_pos[:, :], 0.5)
            nc.gpsimd.memset(ln_eps[:, :], LN_EPS)
            nc.gpsimd.memset(h_scale[:, :], H_SCALE)
            nc.gpsimd.memset(h_scale_neg[:, :], -H_SCALE)
            nc.gpsimd.memset(ident[:, :], 0.0).then_inc(consts_ready, 1)
            pool.wait_ge(consts_ready, 1)
            nc.gpsimd.affine_select(out=ident[:, :], in_=ident[:, :], compare_op=ALU.not_equal, fill=1.0, base=0,
                                    pattern=[[-1, P]], channel_multiplier=1).then_inc(ident_ready, 1)
            nc.gpsimd.affine_select(out=ident16[:, :], in_=ident16[:, :], compare_op=ALU.not_equal, fill=1.0, base=0,
                                    pattern=[[-1, P]], channel_multiplier=1)
            steps = [0]

            def step(ins):
                steps[0] += 1
                ins.then_inc(pool_step, 1)
                return steps[0]

            def layernorm(b, i):
                s = ln[:, i, :]
                pool.wait_ge(stats_ready, nth(T, b, i))
                k = step(nc.gpsimd.tensor_tensor(s[:, 0:1], mv[:, i, 1:2], ln_eps[:, :], ALU.add))
                pool.wait_ge(pool_step, base(b) + k)
                k = step(nc.gpsimd.tensor_tensor(s[:, 0:1], s[:, 0:1], half_neg[:, :], ALU.pow))
                pool.wait_ge(pool_step, base(b) + k)
                nc.gpsimd.tensor_tensor(s[:, 1:2], s[:, 0:1], h_scale[:, :], ALU.mult)
                k = step(nc.gpsimd.tensor_tensor(s[:, 2:3], s[:, 0:1], h_scale_neg[:, :], ALU.mult))
                pool.wait_ge(pool_step, base(b) + k)
                nc.gpsimd.tensor_tensor(s[:, 3:4], mv[:, i, 0:1], s[:, 2:3], ALU.mult).then_inc(ln_ready, 1)

            def base(b):
                return b * (3 * T)

            def all_max(w):
                pool.wait_ge(wmax_ready, w + 1)
                nc.gpsimd.partition_all_reduce(wall[:, w:w + 1], wmax[:, w:w + 1], P,
                                               bass.bass_isa.ReduceOp.max).then_inc(wall_ready, 1)

            for i in range(2):
                layernorm(0, i)
            all_max(0)
            for i in range(2, T):
                layernorm(0, i)
            all_max(1)
            nc.gpsimd.memset(spread[:, :, :], 0.0).then_inc(spread_step, 1)
            for q in range(3):
                pool.wait_ge(spread_step, q + 1)
                nc.gpsimd.affine_select(out=spread[:, :, :], in_=spread[:, :, :], compare_op=ALU.not_equal, fill=1.0,
                                        base=-2 * T * q, pattern=[[-1, 2 * T], [0, P]],
                                        channel_multiplier=1).then_inc(spread_step, 1)
            all_max(2)
            pool.wait_ge(adj_loaded, 16)
            for i in range(T):
                d = adjm[:, i, i * P:(i + 1) * P]
                nc.gpsimd.affine_select(out=d, in_=d, compare_op=ALU.not_equal, fill=0.0, base=0,
                                        pattern=[[-1, P]], channel_multiplier=1).then_inc(adj_ready, 1)

            def batch(b, last):
                pool.wait_ge(sq_ready, nth(1, b, 0))
                nc.gpsimd.tensor_tensor(nrm[:, :], sq[:, L, :], half_pos[:, :], ALU.pow).then_inc(nrm_ready, 1)
                if not last:
                    steps[0] = 0
                    for i in range(T):
                        layernorm(b + 1, i)

            with pool.Fori(0, B - 1) as b:
                batch(b, False)
            batch(B - 1, True)

        @block.scalar
        def _(act):
            def high(kind, b, k, where):
                act.wait_ge(full[kind], nth(COUNT[kind], b, k))
                nc.scalar.activation(split_target(kind, k, HI), split_source(kind, where), ACT.Copy).then_inc(hi_ready[kind], 1)

            def make_h(b, i, t):
                act.wait_ge(ln_ready, nth(T, b, i))
                nc.scalar.activation(t, t, ACT.Relu, bias=ln[:, i, 3:4],
                                     scale=ln[:, i, 1:2]).then_inc(h_ready, 1)

            act.wait_ge(gs_loaded, 32)
            nc.scalar.activation(gexp[:, 0:1], gs[:, 0:1], ACT.Exp, scale=-1.0)
            nc.scalar.activation(gexp[:, 1:2], gs[:, 1:2], ACT.Exp).then_inc(gexp_ready, 1)
            def high_weights(w):
                act.wait_ge(wscale_ready, w + 1)
                for k in range(KC):
                    act.wait_ge(wt_full, w * KC + k + 1)
                    nc.scalar.activation(W[w][:, HI, k, :], w_bank[k][:, :], ACT.Copy, scale=wsc[:, w:w + 1]).then_inc(wt_hi, 1)

            make_h(0, 0, x0[:, 0, :])
            make_h(0, 1, x0[:, 1, :])
            for kind, k in first:
                if (kind, k) == ("h", 2):
                    high_weights(0)
                high(kind, 0, k, FIRST[kind, k][0])
                if kind == "h" and k + 2 < T:
                    make_h(0, k + 2, x0[:, k + 2, :])
                if (kind, k) == ("z", KC):
                    high_weights(1)
                if (kind, k) == ("z", ZT // 2):
                    for c in range(KC):
                        act.wait_ge(wt_full, 2 * KC + c + 1)
                        nc.scalar.activation(woT[:, c, :], w_bank[c][:, :], ACT.Copy).then_inc(woT_ready, 1)
            for k in range(KC):
                act.wait_ge(wvo_full, k + 1)
                nc.scalar.activation(wvo[:, k, :], w_bank[k][:, :], ACT.Copy).then_inc(wvo_ready, 1)
            act.wait_ge(wscale_ready, 3)
            for k in range(KC):
                nc.scalar.activation(W[2][:, HI, k, :], wvo[:, k, :], ACT.Copy, scale=wsc[:, 2:3]).then_inc(wt_hi, 1)

            def batch(b, last):
                where = RING[last]
                for k in range(DG):
                    act.wait_ge(full["diag"], nth(DG, b, k))
                    m, i0 = k * HB // T, k * HB % T
                    for i in range(HB):
                        ins = nc.scalar.activation(tri_at(m, i0 + i, i0 + i, 1), where["diag", k][0][:, i * P:(i + 1) * P], ACT.Copy)
                    ins.then_inc(diag_copied, 1)
                for kind, k in order(last)[DG:]:
                    if kind == "v":
                        if k == last_before_rows(last):
                            act.wait_ge(colT_full, nth(1, b, 0))
                            nc.scalar.activation(colT[:, :], colT_bank[:, 0:P // 2].bitcast(BF16), ACT.Copy).then_inc(colT_ready, 1)
                        if last and k == T - V_LATE:
                            exp_row(b, T - 1)
                            high_row(b, 1)
                        high("v", b, k, where["v", k][0])
                        if last and k == T - 1:
                            scale_language(b, 2)
                    if kind == "row":
                        act.wait_ge(full["row"], nth(RW, b, k))
                        m, hf = k // HALF, k % HALF
                        nc.scalar.activation(rows[:, m, hf * BANK:(hf + 1) * BANK], where["row", k][0][:, :], ACT.Copy).then_inc(row_copied, 1)
                        if k == RW - 1 and not last:
                            make_h(b + 1, 0, xl[:, 0, :])
                    if kind == "h":
                        high("h", b + 1, k, where["h", k][0])
                        if k + 1 < T:
                            make_h(b + 1, k + 1, xl[:, (k + 1) % XL, :])
                    if kind == "off" and ends_row(k):
                        exp_row(b, off_pieces[k][1])
                    if kind == "off" and k in SCALE_AT:
                        scale_language(b, SCALE_AT[k])
                    if kind == "off" and last and k == SPLIT0_AT:
                        high_row(b, 0)
                if not last:
                    exp_row(b, T - 1)
                ahead = rows_ahead(last)
                for s in range(T + 1):
                    if s < T and not last:
                        high_row(b, s)
                        high("z", b + 1, 2 * s, where["z", 2 * s][0])
                    if 0 < s < T - 1 and last:
                        high_row(b, s + 1)
                    for k in z_behind(s):
                        if not last:
                            high("z", b + 1, k, where["z", k][0])
                    if s + ahead < T:
                        scale_language(b, s + ahead)

            def high_row(b, i):
                act.wait_ge(k_ready, nth(T, b, i))
                if i > 0:
                    act.wait_ge(k_written, 16 * nth(T, b, i - 1))
                nc.scalar.activation(kn[:, :, :, HI, :], squares(i), ACT.Copy).then_inc(k_hi, 1)

            def scale_language(b, i):
                act.wait_ge(wr_ready, nth(T, b, i))
                nc.scalar.activation(masked(L, i), masked(L, i), ACT.Copy, scale=wr[:, i % 2, L:L + 1]).then_inc(lscaled, 1)

            def exp_row(b, i):
                if i < T - 1:
                    act.wait_ge(off_done, nth(OFF, b, max(k for k in range(OFF) if off_pieces[k][1] == i)))
                else:
                    act.wait_ge(corner_done, nth(1, b, 0))
                t = tri_at(G, i, i, T - i)
                nc.scalar.activation(t, t, ACT.Exp, scale=beta[:, 0:1]).then_inc(exp_ready, 1)

            act.wait_ge(scal_ready, 1)
            with act.Fori(0, B - 1) as b:
                batch(b, False)
            batch(B - 1, True)

        @block.vector
        def _(dve):
            steps = [0, 0]

            def link(ins, b=None):
                steps[1 if b is not None else 0] += 1
                ins.then_inc(vec_step, 1)
                if b is None:
                    dve.wait_ge(vec_step, steps[0])
                else:
                    dve.wait_ge(vec_step, b * LINKS + (steps[0] + steps[1]))

            def low(kind, b, k, where):
                dve.wait_ge(hi_ready[kind], nth(COUNT[kind], b, k))
                nc.vector.tensor_tensor(split_target(kind, k, LO), split_source(kind, where), split_target(kind, k, HI),
                                        ALU.subtract).then_inc(lo_ready[kind], 1)

            def statistics(i, b=None):
                if b is None:
                    dve.wait_ge(x0_loaded[i // 2], 16)
                else:
                    dve.wait_ge(xl_loaded[i % XL], 16 * nth(T // XL, b, i // XL))
                link(nc.vector.bn_stats(stats[:, i, :], x0[:, i, :] if b is None else xl[:, i % XL, :]), b)
                nc.vector.memset(spare[:, :], 0.0)
                nc.vector.bn_aggr(mv[:, i, :], stats[:, i, :]).then_inc(stats_ready, 1)

            def scale_of(w):
                dve.wait_ge(wall_ready, w + 1)
                c = slice(w, w + 1)
                link(nc.vector.tensor_scalar_max(wpow[:, c], wall[:, c], 1e-30))
                link(nc.vector.tensor_single_scalar(wpow[:, c].bitcast(I32), wpow[:, c].bitcast(I32), 0x7F800000, ALU.bitwise_and))
                link(nc.vector.tensor_scalar(winv[:, c].bitcast(I32), wpow[:, c].bitcast(I32), -1.0, float(0x7F000000), ALU.mult, ALU.add))
                nc.vector.tensor_scalar_mul(wun[:, c], wpow[:, c], 1.0 / (W_SCALE * H_SCALE))
                nc.vector.tensor_scalar_mul(wsc[:, c], winv[:, c], W_SCALE).then_inc(wscale_ready, 1)

            def low_weights(w, k, src):
                dve.wait_ge(wt_hi, w * KC + k + 1)
                nc.vector.scalar_tensor_tensor(W[w][:, LO, k, :], src, wsc[:, w:w + 1], W[w][:, HI, k, :], ALU.mult, ALU.subtract).then_inc(wt_lo, 1)

            def largest(w, src):
                nc.vector.tensor_reduce(wmax[:, w:w + 1], src, AX.XY, ALU.max, apply_absolute_value=True).then_inc(wmax_ready, 1)

            def split_weights(w):
                for k in range(KC):
                    low_weights(w, k, w_bank[k][:, :])

            nc.vector.memset(col_part[:, :], 0.0)
            for i in range(2):
                statistics(i)
            dve.wait_ge(w_loaded[0], 16)
            largest(0, w_raw[0])
            for i in range(2, 4):
                statistics(i)
            scale_of(0)
            for kind, k in first:
                if (kind, k) == ("h", 2):
                    split_weights(0)
                low(kind, 0, k, FIRST[kind, k][0])
                if kind == "h" and k + 4 < T:
                    statistics(k + 4)
                if (kind, k) == ("h", T // 2 - 1):
                    dve.wait_ge(w_loaded[1], 16)
                    largest(1, w_raw[1])
                if (kind, k) == ("z", KC - 1):
                    scale_of(1)
                if (kind, k) == ("z", KC):
                    split_weights(1)
            dve.wait_ge(wvo_ready, KC)
            largest(2, wvo)
            dve.wait_ge(gexp_ready, 1)
            link(nc.vector.tensor_scalar_add(gtmp[:, 0:1], gexp[:, 0:1], 1.0))
            link(nc.vector.reciprocal(gtmp[:, 1:2], gtmp[:, 0:1]))
            link(nc.vector.tensor_scalar_mul(wk[:, L:L + 1], gtmp[:, 1:2], K_SCALE))
            link(nc.vector.tensor_scalar(wk[:, G:G + 1], wk[:, L:L + 1], -1.0, K_SCALE, ALU.mult, ALU.add))
            link(nc.vector.tensor_tensor(gtmp[:, 2:3], gexp[:, 1:2], gexp[:, 1:2], ALU.mult))
            link(nc.vector.reciprocal(gtmp[:, 3:4], gtmp[:, 2:3]))
            nc.vector.tensor_scalar(beta[:, :], gtmp[:, 3:4], wun[:, G:G + 1], wun[:, G:G + 1], ALU.mult, ALU.mult).then_inc(scal_ready, 1)
            scale_of(2)
            for k in range(KC):
                low_weights(2, k, wvo[:, k, :])
            link(nc.vector.tensor_scalar_mul(vun[:, :], wun[:, 2:3], 1.0 / K_SCALE))
            dve.wait_ge(adj_ready, T)
            link(nc.vector.memset(part[:, :, :, :], 0.0))

            def mask(b, i, m, last):
                scalar, op = ((0.0, ALU.max), (1.0, ALU.min))[m]
                for piece, (pm, pi, j, n) in enumerate(raw_pieces):
                    if (pm, pi) == (m, i):
                        dve.wait_ge(raw_full, nth(RAW, b, piece))
                        nc.vector.scalar_tensor_tensor(masked(m, i)[:, j * P:(j + n) * P], raw_at(piece, last)[0][:, 0:n * P], scalar,
                                                       adjm[:, i, j * P:(j + n) * P], op, ALU.mult,
                                                       accum_out=part[:, i, m, j // HB:j // HB + 1]).then_inc(raw_masked, 1)
                if m == G:
                    dve.wait_ge(exp_ready, nth(T, b, i))
                ins = nc.vector.scalar_tensor_tensor(masked(m, i)[:, i * P:N], tri_at(m, i, i, T - i), scalar,
                                                     adjm[:, i, i * P:N], op, ALU.mult, accum_out=part[:, i, m, 2:3])
                if m == G:
                    r = i % 2
                    link(ins, b)
                    link(nc.vector.reduce_sum(deg[:, r, :], part[:, i, :, :], AX.X), b)
                    link(nc.vector.tensor_scalar_max(deg[:, r, :], deg[:, r, :], EPS), b)
                    link(nc.vector.reciprocal(deg[:, r, :], deg[:, r, :]), b)
                    nc.vector.tensor_tensor(wr[:, r, :], deg[:, r, :], wk[:, :], ALU.mult).then_inc(wr_ready, 1)

            def combine(b, i):
                dve.wait_ge(lscaled, nth(T, b, i))
                nc.vector.scalar_tensor_tensor(masked(L, i), masked(G, i), wr[:, i % 2, G:G + 1], masked(L, i),
                                               ALU.mult, ALU.add).then_inc(k_combined, 1)
                dve.wait_ge(k_combined, nth(T, b, i))
                nc.vector.transpose(squares(i).rearrange("p b n j -> p j b n"),
                                    masked(L, i).rearrange("p (j b m) -> p j b m", j=T, b=NQ)).then_inc(k_ready, 1)

            def low_row(b, i):
                dve.wait_ge(k_hi, nth(T, b, i))
                nc.vector.tensor_tensor(kn[:, :, :, LO, :], squares(i), kn[:, :, :, HI, :], ALU.subtract).then_inc(k_split, 1)

            def batch(b, last):
                where = RING[last]
                steps[1] = 0
                for m in (L, G):
                    for i in range(T):
                        if i % HB == 0:
                            dve.wait_ge(diag_copied, nth(DG, b, (m * T + i) // HB))
                        ins = nc.vector.scalar_tensor_tensor(masked(m, 0)[:, i * P:(i + 1) * P], tri_at(m, i, i, 1), 1.0, ident[:, :], ALU.mult, ALU.mult,
                                                             accum_out=sq[:, m, i:i + 1])
                    if m == L:
                        ins.then_inc(sq_ready, 1)
                low("v", b, 0, where["v", 0][0])
                dve.wait_ge(nrm_ready, nth(1, b, 0))
                link(nc.vector.tensor_scalar(nrm[:, :], nrm[:, :], wun[:, L:L + 1], EPS, ALU.mult, ALU.max), b)
                link(nc.vector.reciprocal(nrm[:, :], nrm[:, :]), b)
                nc.vector.tensor_scalar(col[:, L, :], nrm[:, :], wun[:, L:L + 1], None, ALU.mult)
                link(nc.vector.tensor_scalar_mul(col[:, G, :], sq[:, G, :], 0.5), b)
                low("v", b, 1, where["v", 1][0])
                C = 2 * T
                rest = col[:, :, :].rearrange("p m t -> p (m t)")
                for q in range(2):
                    link(nc.vector.tensor_copy(col_part[:, q * C:(q + 1) * C], rest), b)
                    link(nc.vector.tensor_tensor(col_rest[:, q, :], rest, col_part[:, q * C:(q + 1) * C], ALU.subtract), b)
                    rest = col_rest[:, q, :]
                nc.vector.tensor_copy(col_part[:, 2 * C:3 * C], rest).then_inc(colpart_ready, 1)
                low("v", b, 2, where["v", 2][0])
                if not last:
                    statistics(0, b)
                    statistics(1, b)

                def finish(m, i, j, n, src):
                    op = ALU.mult if m == L else ALU.subtract
                    return nc.vector.scalar_tensor_tensor(tri_at(m, i, j, n), src, col[:, m, i:i + 1], rows[:, m, j * P:(j + n) * P], op, op)

                def corner(b):
                    finish(L, T - 1, T - 1, 1, tri_at(L, T - 1, T - 1, 1))
                    finish(G, T - 1, T - 1, 1, tri_at(G, T - 1, T - 1, 1)).then_inc(corner_done, 1)
                    dve.wait_ge(corner_done, nth(1, b, 0))

                for kind, k in order(last)[DG + 3:]:
                    if kind == "v":
                        if last and k == T - V_LATE:
                            corner(b)
                            combine(b, 1)
                            low_row(b, 1)
                        low("v", b, k, where["v", k][0])
                        if k in late_v(last):
                            mask(b, 2, late_v(last)[k], last)
                        if last and k == T - 1:
                            combine(b, 2)
                    if kind == "row" and k == RW - 1:
                        dve.wait_ge(row_copied, nth(RW, b, RW - 1))
                    if kind == "off":
                        m, i, j, n = off_pieces[k]
                        if j == i + 1:
                            finish(m, i, i, 1, tri_at(m, i, i, 1))
                        dve.wait_ge(full["off"], nth(OFF, b, k))
                        ins = finish(m, i, j, n, where["off", k][0][:, 0:n * P])
                        ins.then_inc(off_done, 1)
                        if k in MASK_AT:
                            mask(b, *MASK_AT[k], last)
                        if k in COMBINE_AT:
                            combine(b, COMBINE_AT[k])
                        if last and k == SPLIT0_AT:
                            low_row(b, 0)
                    if kind == "h":
                        low("h", b + 1, k, where["h", k][0])
                        if k + 2 < T:
                            statistics(k + 2, b)
                if not last:
                    corner(b)
                    combine(b, 1)
                ahead = rows_ahead(last)
                for s in range(T + 1):
                    if s < T:
                        if not last:
                            low_row(b, s)
                            low("z", b + 1, 2 * s, where["z", 2 * s][0])
                        if s + ahead < T:
                            mask(b, s + ahead, L, last)
                        if s + ahead < T and last:
                            mask(b, s + ahead, G, last)
                        if 0 < s < T - 1 and last:
                            low_row(b, s + 1)
                        if s + ahead < T and last:
                            combine(b, s + ahead)
                    for k in z_behind(s):
                        if not last:
                            low("z", b + 1, k, where["z", k][0])
                    if s + ahead < T and not last:
                        mask(b, s + ahead, G, last)
                        combine(b, s + ahead)
                    if s > 0:
                        i = s - 1
                        dve.wait_ge(kv_full, nth(T, b, i))
                        dve.wait_ge(xr_loaded[i % 2], 16 * nth(T // 2, b, i // 2))
                        nc.vector.scalar_tensor_tensor(xr[:, i % 2, :], product_bank(i, last)[:, :], vun[:, 0:1], xr[:, i % 2, :],
                                                       ALU.mult, ALU.add).then_inc(out_ready, 1)

            LINKS = T + 3 + 4 + 4 * T
            with dve.Fori(0, B - 1) as b:
                batch(b, False)
            assert steps[1] == LINKS
            batch(B - 1, True)

        @block.tensor
        def _(pe):
            def transpose(dst, src):
                return nc.tensor.transpose(dst, src, ident[:, :])

            def free_of(before, b):
                kind, k, back = before
                pe.wait_ge(FREED[kind], nth(COUNT[kind], batch_of(kind, b) + back, k))

            def product(dst, pairs):
                n = len(pairs) * len(PASSES)
                at = 0
                for lhs, rhs in pairs:
                    for pl, pr in PASSES:
                        last = nc.tensor.matmul(dst, lhs(pl), rhs(pr), start=at == 0, stop=at == n - 1)
                        at += 1
                return last

            def h_piece(b, k, where, src):
                pe.wait_ge(h_ready, nth(T, b, k))
                for c in range(KC):
                    last = transpose(where[:, c * P:(c + 1) * P], src[:, c * P:(c + 1) * P])
                last.then_inc(full["h"], 1)

            def z_piece(b, k, where):
                m, e, hf = z_tile(k)
                last = product(where[:, :], [(lambda p, c=c: W[m][:, p, c, e * P:(e + 1) * P],
                                              lambda p, c=c: hT[:, p, c, hf * BANK:(hf + 1) * BANK]) for c in range(KC)])
                last.then_inc(full["z"], 1)

            def v_piece(b, k, where):
                last = product(where[:, :], [(lambda p, c=c: hT[:, p, c, k * P:(k + 1) * P],
                                              lambda p, c=c: W[2][:, p, c, :]) for c in range(KC)])
                last.then_inc(full["v"], 1)

            def gram(m, i, j, n, dst):
                return product(dst, [(lambda p, c=c: zT[m][:, p, c, i * P:(i + 1) * P],
                                      lambda p, c=c: zT[m][:, p, c, j * P:(j + n) * P]) for c in range(KC)])

            def transpose_weights(w):
                pe.wait_ge(w_loaded[w], 16)
                for k in range(KC):
                    if w:
                        pe.wait_ge(wt_lo, (w - 1) * KC + k + 1)
                    for c in range(KC):
                        last = transpose(w_bank[k][:, c * P:(c + 1) * P], w_raw[w][:, c, k * P:(k + 1) * P])
                    last.then_inc(wt_full, 1)

            pe.wait_ge(ident_ready, 1)
            transpose_weights(0)
            for kind, k in first:
                if (kind, k) == ("z", 0):
                    pe.wait_ge(wt_lo, KC)
                if (kind, k) == ("z", KC):
                    transpose_weights(1)
                if (kind, k) == ("z", ZT // 2):
                    transpose_weights(2)
                where, before = FIRST[kind, k]
                if before:
                    free_of(before, 0)
                if kind == "h":
                    h_piece(0, k, where, x0[:, k, :])
                else:
                    if k % KC == 0:
                        pe.wait_ge(lo_ready["h"], T // 2 if k == 0 else T)
                    z_piece(0, k, where)
            pe.wait_ge(w_loaded[3], 16)
            pe.wait_ge(woT_ready, KC)
            for k in range(KC):
                for f in range(KC):
                    last = nc.tensor.matmul(w_bank[k][:, :], w_raw[3][:, f, k * P:(k + 1) * P], woT[:, f, :],
                                            start=f == 0, stop=f == KC - 1)
                last.then_inc(wvo_full, 1)
            pe.wait_ge(spread_step, 4)

            def batch(b, last_batch):
                where = RING[last_batch]

                def take(kind, k):
                    bank_, before = where[kind, k]
                    free_of(before, b)
                    return bank_

                def raws(m, i):
                    for piece, (pm, pi, j, n) in enumerate(raw_pieces):
                        if (pm, pi) == (m, i):
                            raw, before = raw_at(piece, last_batch)
                            if before is not None:
                                pe.wait_ge(raw_masked, nth(RAW, b, before))
                            if m == L:
                                pe.wait_ge(off_done, nth(OFF, b, 0 if i == 1 else OFF - 1))
                            if m == G:
                                pe.wait_ge(exp_ready, nth(T, b, j + n - 1))
                            for q in range(n):
                                last = transpose(raw[:, q * P:(q + 1) * P], tri_at(m, j + q, i, 1))
                            last.then_inc(raw_full, 1)

                for kind, k in order(last_batch):
                    if (kind, k) == ("v", last_before_rows(last_batch)):
                        pe.wait_ge(colpart_ready, nth(1, b, 0))
                        nc.tensor.transpose(colT_bank[:, 0:P // 2].bitcast(BF16), col_part[:, :], ident16[:, :]).then_inc(colT_full, 1)
                    if kind == "row" and k == 0:
                        pe.wait_ge(colT_ready, nth(1, b, 0))
                    bank_ = take(kind, k)
                    if kind == "diag":
                        m, i0 = k * HB // T, k * HB % T
                        if i0 == 0:
                            pe.wait_ge(lo_ready["z"], nth(ZT, b, (m + 1) * ZT // 2 - 1))
                        for i in range(HB):
                            last = gram(m, i0 + i, i0 + i, 1, bank_[:, i * P:(i + 1) * P])
                        last.then_inc(full["diag"], 1)
                    if kind == "v":
                        if k == 0:
                            pe.wait_ge(wt_lo, 3 * KC)
                        v_piece(b, k, bank_)
                    if kind == "row":
                        for c in range(HB):
                            last = nc.tensor.matmul(bank_[:, c * P:(c + 1) * P], spread[:, k * HB + c, :], colT[:, :],
                                                    start=True, stop=True)
                        last.then_inc(full["row"], 1)
                    if kind == "off":
                        m, i, j, n = off_pieces[k]
                        gram(m, i, j, n, bank_[:, 0:n * P]).then_inc(full["off"], 1)
                        if k == RAW1_AT:
                            raws(L, 1)
                            raws(G, 1)
                    if kind == "v" and k in late_v(last_batch):
                        raws(late_v(last_batch)[k], 2)
                    if kind == "h":
                        h_piece(b + 1, k, bank_, xl[:, k % XL, :])

                def z_next(k):
                    if not last_batch:
                        if k == 0:
                            pe.wait_ge(lo_ready["h"], nth(T, b + 1, T - 1))
                        z_piece(b + 1, k, take("z", k))

                def aggregate(i):
                    turns = 2 if last_batch else 1
                    if i >= turns:
                        pe.wait_ge(out_ready, nth(T, b, i - turns))
                    if i == 0 and not last_batch:
                        pe.wait_ge(lo_ready["v"], nth(T, b, T - 1))
                    pe.wait_ge(kt_ready[i % 2], 16 * NQ * nth(T // 2, b, i // 2))
                    at = 0
                    for j in range(T):
                        for pl, pr in PASSES:
                            last = nc.tensor.matmul(product_bank(i, last_batch)[:, :], KT[:, i % 2, :, pl, j], v[:, pr, j, :], start=at == 0,
                                                    stop=at == T * len(PASSES) - 1)
                            at += 1
                    last.then_inc(kv_full, 1)

                ahead = rows_ahead(last_batch)
                for s in range(T + 1):
                    if s == 1 and last_batch:
                        pe.wait_ge(lo_ready["v"], nth(T, b, T - 1))
                    if s < T:
                        z_next(2 * s)
                        if s + ahead < T:
                            raws(L, s + ahead)
                    for k in z_behind(s):
                        z_next(k)
                    if s + ahead < T:
                        raws(G, s + ahead)
                    if s > 0:
                        aggregate(s - 1)

            with pe.Fori(0, B - 1) as b:
                batch(b, False)
            batch(B - 1, True)


_INS = ["x", "adj", "L0_gnn_W_lang", "L0_gnn_W_grav", "L0_gnn_W_V", "L0_gnn_W_O", "L0_gnn_gate_logit", "L0_gnn_log_sigma"]


def kernel(**inputs):
    import concourse.bacc as bacc
    from concourse.bass_utils import run_bass_kernel_spmd

    nc = bacc.Bacc("TRN2", target_bir_lowering=False, num_devices=1)
    arrays, args = {}, []
    for name in _INS:
        a = np.ascontiguousarray(inputs[name])
        if a.ndim == 0:
            a = a.reshape(1)
        arrays[f"in_{name}_dram"] = a
        args.append(nc.dram_tensor(f"in_{name}_dram", a.shape, mybir.dt.from_np(a.dtype), kind="ExternalInput").ap())
    x = inputs["x"]
    args.append(nc.dram_tensor("out_0_dram", x.shape, F32, kind="ExternalOutput").ap())
    gnn_kernel(nc, *args)
    r = run_bass_kernel_spmd(nc, [arrays], core_ids=[0])
    return r.results[0]["out_0_dram"]
```
